# Optimizing a Trainium2 kernel written in Bass

```python
import numpy as np
import jax
import jax.numpy as jnp

def _softmax(x, axis=-1):
    return jax.nn.softmax(x, axis=axis)
def _gelu(x):
    return jax.nn.gelu(x, approximate=True)
def _silu(x):
    return jax.nn.silu(x)
def _sigmoid(x):
    return jax.nn.sigmoid(x)
def _layernorm(x, axis=-1, eps=1e-5):
    m = jnp.mean(x, axis=axis, keepdims=True)
    v = jnp.var(x, axis=axis, keepdims=True)
    return (x - m) / jnp.sqrt(v + eps)
def _scatter_add(tgt, idx, src, axis=0):
    return tgt.at[idx].add(src)
def _segment_sum(src, seg, n):
    return jax.ops.segment_sum(src, seg, n)

kernel_name = 'mk_conv_preact_d2_conv_nhwc256_b5a441'

def setup_inputs(seed: int = 0):
    np.random.seed(seed)
    _w = jnp.asarray
    def _rec_inputs():
        import jax
        import jax.numpy as jnp
        _gk = jax.random.key(seed)
        x = -8.268e-05 + 0.9999 * jax.random.normal(jax.random.fold_in(_gk, 1), (16, 112, 112, 256), jnp.float32)
        return x
    x = _rec_inputs()
    def _L0_conv_setup():
        import jax, jax.numpy as jnp
        import numpy as np

        @jax.custom_vjp
        def ste_sign(x):
            return jnp.where(x >= 0, jnp.ones((), x.dtype), -jnp.ones((), x.dtype))

        def _ste_fwd(x):
            return (ste_sign(x), x)

        def _ste_bwd(x, g):
            return (g * (jnp.abs(x) <= 1).astype(g.dtype),)
        ste_sign.defvjp(_ste_fwd, _ste_bwd)
        key = jax.random.key(seed)
        k1, k2 = jax.random.split(key)
        x = jax.random.normal(k1, (16, 112, 112, 256), dtype=jnp.float32)
        kernel = jax.random.normal(k2, (3, 3, 256, 1), dtype=jnp.float32) * 0.1
        return {'x': x, 'kernel': kernel}
    _L0_conv_all = _L0_conv_setup()
    _L0_conv_in = {k: v for k, v in _L0_conv_all.items() if k in ('kernel', )}
    del _L0_conv_all

    def _L1_conv_setup():
        import jax, jax.numpy as jnp
        import numpy as np

        @jax.custom_vjp
        def ste_sign(x):
            return jnp.where(x >= 0, jnp.ones((), x.dtype), -jnp.ones((), x.dtype))

        def _ste_fwd(x):
            return (ste_sign(x), x)

        def _ste_bwd(x, g):
            return (g * (jnp.abs(x) <= 1).astype(g.dtype),)
        ste_sign.defvjp(_ste_fwd, _ste_bwd)
        key = jax.random.key(seed)
        k1, k2 = jax.random.split(key)
        x = jax.random.normal(k1, (16, 112, 112, 256), dtype=jnp.float32)
        kernel = jax.random.normal(k2, (3, 3, 256, 1), dtype=jnp.float32) * 0.1
        return {'x': x, 'kernel': kernel}
    _L1_conv_all = _L1_conv_setup()
    _L1_conv_in = {k: v for k, v in _L1_conv_all.items() if k in ('kernel', )}
    del _L1_conv_all

    return {
        "x": x,
        "L0_conv_kernel": _L0_conv_in["kernel"],
        "L1_conv_kernel": _L1_conv_in["kernel"],
    }

def reference(x, L0_conv_kernel, L1_conv_kernel):
    import jax
    import jax.numpy as jnp
    def _L0_conv_ref(x, kernel):
        import jax, jax.numpy as jnp
        import numpy as np

        @jax.custom_vjp
        def ste_sign(x):
            return jnp.where(x >= 0, jnp.ones((), x.dtype), -jnp.ones((), x.dtype))

        def _ste_fwd(x):
            return (ste_sign(x), x)

        def _ste_bwd(x, g):
            return (g * (jnp.abs(x) <= 1).astype(g.dtype),)
        ste_sign.defvjp(_ste_fwd, _ste_bwd)
        xq = ste_sign(x)
        kq = ste_sign(kernel)
        kh, kw, C, mult = kernel.shape
        rhs = kq.reshape(kh, kw, 1, C * mult)
        out = jax.lax.conv_general_dilated(xq, rhs, window_strides=(1, 1), padding='SAME', feature_group_count=C, dimension_numbers=('NHWC', 'HWIO', 'NHWC'))
        return out

    def _L1_conv_ref(x, kernel):
        import jax, jax.numpy as jnp
        import numpy as np

        @jax.custom_vjp
        def ste_sign(x):
            return jnp.where(x >= 0, jnp.ones((), x.dtype), -jnp.ones((), x.dtype))

        def _ste_fwd(x):
            return (ste_sign(x), x)

        def _ste_bwd(x, g):
            return (g * (jnp.abs(x) <= 1).astype(g.dtype),)
        ste_sign.defvjp(_ste_fwd, _ste_bwd)
        xq = ste_sign(x)
        kq = ste_sign(kernel)
        kh, kw, C, mult = kernel.shape
        rhs = kq.reshape(kh, kw, 1, C * mult)
        out = jax.lax.conv_general_dilated(xq, rhs, window_strides=(1, 1), padding='SAME', feature_group_count=C, dimension_numbers=('NHWC', 'HWIO', 'NHWC'))
        return out

    def _gn(v, G=32, eps=1e-5):
        B_, H_, W_, C_ = v.shape
        g = v.reshape(B_, H_, W_, G, C_ // G)
        m = jnp.mean(g, axis=(1, 2, 4), keepdims=True)
        s = jnp.var(g, axis=(1, 2, 4), keepdims=True)
        return ((g - m) / jnp.sqrt(s + eps)).reshape(v.shape)

    def _ln_c(v, eps=1e-6):
        m = jnp.mean(v, axis=-1, keepdims=True)
        s = jnp.var(v, axis=-1, keepdims=True)
        return (v - m) / jnp.sqrt(s + eps)

    def _ln_t(v, eps=1e-5):
        m = jnp.mean(v, axis=-1, keepdims=True)
        s = jnp.var(v, axis=-1, keepdims=True)
        return (v - m) / jnp.sqrt(s + eps)

    def _to_tokens(v):
        B_, H_, W_, C_ = v.shape
        return v.reshape(B_, H_ * W_, C_)
    def _from_tokens(t, like):
        return t.reshape(like.shape)

    x = x + _L0_conv_ref(_gn(x), L0_conv_kernel)
    x = x + _L1_conv_ref(_gn(x), L1_conv_kernel)
    return x


_drawn_inputs = setup_inputs


def setup_inputs(seed=0):
    import zlib

    import numpy as np

    out = dict(_drawn_inputs(seed))
    spreads = {}
    factors = {}
    for name, (base, spread) in spreads.items():
        noise = np.random.default_rng([zlib.crc32(name.encode()), seed]).standard_normal(out[name].shape)
        drawn = base * np.exp(spread * noise) if base else spread * noise
        out[name] = jnp.asarray(drawn.astype(out[name].dtype))
    for name, factor in factors.items():
        out[name] = (out[name] * factor).astype(out[name].dtype)
    return out
```

```python
from contextlib import ExitStack

import concourse.bass as bass
from concourse import mybir

ALU = mybir.AluOpType
ACT = mybir.ActivationFunctionType
F32 = mybir.dt.float32
BF16 = mybir.dt.bfloat16
FP8 = mybir.dt.float8e4
U32 = mybir.dt.uint32


N, H, W, C = 16, 112, 112, 256
GROUP = 8
HALVES = 2
CH = C // HALVES
GPU = CH // GROUP
UNITS = HALVES * N
HALF_GROUPS = N * GPU
GROUPS = HALVES * HALF_GROUPS
TAPS = 3
M = 128
PITCH = 113
BANDS = CH * TAPS
GROUP_BANDS = GROUP * TAPS * PITCH
SCRATCH_W = M + BANDS * PITCH + M
COPIES = 16
PC = 128
SLOT = GROUP * PC
PIECES = 4
WP = W // PIECES
BPIECES = 4
BGROUPS = GPU // BPIECES
GUARD = M - PITCH
BPIECE_W = BGROUPS * GROUP_BANDS + GUARD
SUMS = 2
DMA = 16


def band_conv_kernel(nc, x, k0, k1, out):
    band_rows = nc.dram_tensor("band_rows", [2 * HALVES * COPIES, SCRATCH_W], FP8, kind="Internal").ap()

    with ExitStack() as ctx:
        def sb(name, shape, dt):
            return ctx.enter_context(nc.sbuf_tensor(name, shape, dt))

        def pb(name, shape, dt):
            return ctx.enter_context(nc.psum_tensor(name, shape, dt))

        def sem(name):
            return ctx.enter_context(nc.semaphore(name))

        act_x = sb("act_x", [H, 2, W, CH], F32)
        bands = [sb(f"bands{l}", [H, BPIECES * BPIECE_W], FP8) for l in range(2)]
        signs = [sb(f"signs{l}", [H, 2, GROUP, W + 2], BF16) for l in range(2)]
        rowsum = [sb(f"rowsum{l}", [H, SUMS], F32) for l in range(2)]
        averager = sb("averager", [H, M], F32)
        taps = sb("taps", [CH, 2 * HALVES, TAPS * TAPS], F32)
        unread_or_taps = sb("unread_or_taps", [CH, GROUP * W], BF16)
        unread = unread_or_taps[0:H, :].rearrange("h (c w) -> h c w", c=GROUP)
        tap_rows = unread_or_taps[:, :].bitcast(FP8)[:, 0:2 * HALVES * TAPS * PITCH].rearrange(
            "c (s d t) -> c s d t", s=2 * HALVES, d=TAPS)
        zero_rows = sb("zero_rows", [2 * HALVES * COPIES, M], FP8)

        conv_ps = [pb("conv0_ps", [M, 2, GROUP, PC], F32), pb("conv1_ps", [M, 1, GROUP, PC], F32)]
        mean_ps = [pb(f"mean{l}_ps", [M, 512], F32) for l in range(2)]

        taps_loaded = sem("taps_loaded")
        zeros_set = sem("zeros_set")
        taps_signed = sem("taps_signed")
        rows_built = sem("rows_built")
        rows_stored = sem("rows_stored")
        band_loaded = [[sem(f"band{l}_loaded{q}") for q in range(BPIECES)] for l in range(2)]
        constants_set = sem("constants_set")
        loaded = sem("loaded")
        stored = [sem(f"stored{i}") for i in range(PIECES)]
        rowsum_ready = sem("rowsum_ready")
        mean_ready = [sem("mean0_ready"), sem("mean1_ready")]
        sign_ready = [sem("sign0_ready"), sem("sign1_ready")]
        conv_ready = [sem("conv0_ready"), sem("conv1_ready")]
        added = [sem("added0"), sem("added1")]

        by_channel = act_x[:, :, :, :].rearrange("p u w c -> p c (u w)")

        def group_of(g):
            return by_channel[:, bass.ds((g & (GPU - 1)) * GROUP, GROUP),
                              bass.ds((g & (2 * GPU - 1)) // GPU * W, W)]

        block = ctx.enter_context(nc.Block())

        def valid(g):
            return not isinstance(g, int) or 0 <= g < GROUPS

        def later(g, by):
            return not isinstance(g, int) or g >= by

        @block.sync
        def _(sp):
            def piece(dram, half, n, i):
                return dram[n, :, i * WP:(i + 1) * WP, half * CH:(half + 1) * CH]

            def held(u, i):
                return act_x[:, u % 2, i * WP:(i + 1) * WP, :]

            def load(half, n, u, i):
                sp.dma_start(held(u, i), piece(x, half, n, i)).then_inc(loaded, DMA)

            def store(half, n, u, i):
                sp.dma_start(piece(out, half, n, i), held(u, i)).then_inc(stored[i], DMA)

            def turn(half, n, parity, next_half, next_n, nth):
                sp.wait_ge(added[1], (nth + 1) * GPU)
                for i in range(PIECES):
                    store(half, n, parity, i)
                if next_n is None:
                    return
                sp.wait_ge(loaded, (nth + 2) * PIECES * DMA)
                for i in range(PIECES):
                    sp.wait_ge(stored[i], (nth + 1) * DMA)
                    load(next_half, next_n, parity, i)

            for i in range(PIECES):
                load(0, 0, 0, i)
            sp.wait_ge(loaded, PIECES * DMA)
            for i in range(PIECES):
                load(0, 1, 1, i)
            for half in range(HALVES):
                with sp.Fori(0, N // 2 - 1) as pair:
                    for parity in range(2):
                        n = pair * 2 + parity
                        turn(half, n, parity, half, n + 2, n + half * N)
                for parity in range(2):
                    more = half + 1 < HALVES
                    turn(half, N - 2 + parity, parity, half + 1, parity if more else None,
                         half * N + N - 2 + parity)
            for i in range(PIECES):
                sp.wait_ge(stored[i], UNITS * DMA)

        @block.gpsimd
        def _(pool):
            nc.gpsimd.memset(averager[:, :], 1.0 / (H * W * GROUP))
            for l in range(2):
                for edge in (0, W + 1):
                    last = nc.gpsimd.memset(signs[l][:, :, :, edge:edge + 1], 0.0)
            last.then_inc(constants_set, 1)

            for l, k in enumerate((k0, k1)):
                pool.dma_start(taps[:, l * HALVES:(l + 1) * HALVES, :],
                               k.rearrange("(h c) t -> c h t", h=HALVES)).then_inc(taps_loaded, DMA)

            pool.wait_ge(zeros_set, 2)
            pool.dma_start(band_rows[:, 0:M], zero_rows[:, :]).then_inc(rows_stored, DMA)
            pool.dma_start(band_rows[:, SCRATCH_W - M:], zero_rows[:, :]).then_inc(rows_stored, DMA)
            pool.wait_ge(rows_built, TAPS)
            for s in range(2 * HALVES):
                pool.dma_start(
                    band_rows[s * COPIES:(s + 1) * COPIES, M:M + BANDS * PITCH].rearrange("r (c t) -> c r t", c=CH),
                    tap_rows[:, s:s + 1, :, :].rearrange("c s d t -> c s (d t)").to_broadcast(
                        [CH, COPIES, TAPS * PITCH])).then_inc(rows_stored, DMA)
            pool.wait_ge(rows_stored, (2 + 2 * HALVES) * DMA)

            def load_bands(l, half, q):
                row = l * HALVES + half
                for h in range(0, H, COPIES):
                    start = row * COPIES * SCRATCH_W + M + 1 - h + q * BGROUPS * GROUP_BANDS
                    src = bass.AP(band_rows.tensor, start, [[SCRATCH_W - 1, COPIES], [1, BPIECE_W]])
                    pool.dma_start(bands[l][h:h + COPIES, q * BPIECE_W:(q + 1) * BPIECE_W],
                                   src).then_inc(band_loaded[l][q], DMA)

            for q in range(BPIECES):
                for l in range(2):
                    load_bands(l, 0, q)
            for half in range(1, HALVES):
                before = half * HALF_GROUPS - GPU
                for q in range(BPIECES):
                    for l in range(2):
                        pool.wait_ge(conv_ready[l], before + (q + 1) * BGROUPS)
                        load_bands(l, half, q)

        @block.scalar
        def _(act):
            act.wait_ge(rows_stored, (2 + 2 * HALVES) * DMA)

            def sum_rows(g, slot):
                act.wait_ge(loaded, (g // GPU + 1) * PIECES * DMA)
                if not isinstance(g, int):
                    act.wait_ge(mean_ready[0], g - (SUMS - 1))
                if later(g, 1):
                    act.wait_ge(rowsum_ready, g)
                nc.scalar.activation(unread, group_of(g), ACT.Copy,
                                     accum_out=rowsum[0][:, slot:slot + 1]).then_inc(rowsum_ready, 1)

            for g in range(SUMS):
                sum_rows(g, g)
            with act.Fori(SUMS, GROUPS, SUMS) as g0:
                for slot in range(SUMS):
                    sum_rows(g0 + slot, slot)

        def steps(eng, step, per_turn):
            first = 2
            last = GROUPS - 2 - (GROUPS - 2 - first) % per_turn
            for t in range(-2, first):
                step(t, t % per_turn)
            with eng.Fori(0, (last - first) // per_turn) as turn:
                for i in range(first, first + per_turn):
                    step(turn * per_turn + i, i % per_turn)
            for t in range(last, GROUPS + 2):
                step(t, t % per_turn)

        @block.vector
        def _(dve):
            nc.vector.memset(zero_rows[:, :], 0.0).then_inc(zeros_set, 1)
            nc.vector.memset(tap_rows[:, :, :, :], 0.0).then_inc(zeros_set, 1)
            dve.wait_ge(taps_loaded, 2 * DMA)
            nc.vector.tensor_scalar(taps[:, :, :], taps[:, :, :], 0.0, 0.5,
                                    ALU.is_ge, ALU.subtract).then_inc(taps_signed, 1)
            dve.wait_ge(taps_signed, 1)
            dve.wait_ge(zeros_set, 2)
            for dy in range(TAPS):
                nc.vector.tensor_scalar(tap_rows[:, :, :, TAPS - 1 - dy], taps[:, :, dy * TAPS:(dy + 1) * TAPS],
                                        4.0, None, ALU.mult, saturate=False).then_inc(rows_built, 1)
            dve.wait_ge(constants_set, 1)

            def sign(l, g, parity):
                dve.wait_ge(mean_ready[l], g + 1)
                if later(g, 2):
                    dve.wait_ge(conv_ready[l], g - 1)
                nc.vector.tensor_scalar(signs[l][:, parity, :, 1:W + 1], group_of(g), mean_ps[l][0:H, 0:1], 0.5,
                                        ALU.is_ge, ALU.subtract).then_inc(sign_ready[l], 1)

            def add(l, g, parity, slot):
                dve.wait_ge(conv_ready[l], g + 1)
                here = group_of(g)
                if l == 0:
                    nc.vector.scalar_tensor_tensor(here, conv_ps[0][0:H, parity, :, 0:W], 0.0, here,
                                                   ALU.add, ALU.add,
                                                   accum_out=rowsum[1][:, slot:slot + 1]).then_inc(added[0], 1)
                else:
                    nc.vector.tensor_tensor(here, conv_ps[1][0:H, 0, :, 0:W], here, ALU.add).then_inc(added[1], 1)

            def step(t, parity):
                if valid(t + 1):
                    sign(0, t + 1, 1 - parity)
                if valid(t):
                    add(0, t, parity, parity)
                if valid(t - 1):
                    sign(1, t - 1, 1 - parity)
                if valid(t - 2):
                    add(1, t - 2, parity, None)

            steps(dve, step, 2)

        @block.tensor
        def _(pe):
            pe.wait_ge(constants_set, 1)

            def mean(l, g, slot):
                pe.wait_ge(rowsum_ready if l == 0 else added[0], g + 1)
                if later(g, 1):
                    pe.wait_ge(sign_ready[l], g)
                nc.tensor.matmul(mean_ps[l][:, 0:1], averager[:, :], rowsum[l][:, slot:slot + 1],
                                 start=True, stop=True).then_inc(mean_ready[l], 1)

            def conv_waits(l, g, gi):
                q, in_piece = divmod(gi, BGROUPS)
                if in_piece == 0:
                    pe.wait_ge(band_loaded[l][q], (g // HALF_GROUPS + 1) * (H // COPIES) * DMA)
                slots = 2 - l
                if later(g, slots):
                    pe.wait_ge(added[l], g - slots + 1)
                pe.wait_ge(sign_ready[l], g + 1)

            def conv(l, gi):
                q, in_piece = divmod(gi, BGROUPS)
                slots = 2 - l
                for c in range(GROUP):
                    for dx in range(TAPS):
                        at = q * BPIECE_W + ((in_piece * GROUP + c) * TAPS + dx) * PITCH
                        last = nc.tensor.matmul(
                            conv_ps[l][:, gi % slots, c, 0:W],
                            bands[l][:, at:at + M],
                            signs[l][:, gi % 2, c, dx:dx + W],
                            start=(dx == 0), stop=(dx == TAPS - 1))
                last.then_inc(conv_ready[l], 1)

            def step(t, i):
                if valid(t - 2):
                    conv_waits(1, t - 2, (i - 2) % GPU)
                if valid(t - 1):
                    mean(1, t - 1, (i - 1) % 2)
                if valid(t - 2):
                    conv(1, (i - 2) % GPU)
                if valid(t + 1):
                    conv_waits(0, t + 1, (i + 1) % GPU)
                if valid(t + 2):
                    mean(0, t + 2, i % 2)
                if valid(t + 1):
                    conv(0, (i + 1) % GPU)

            steps(pe, step, GPU)


_INS = ["x", "L0_conv_kernel", "L1_conv_kernel"]
_OUTS = [((N, H, W, C), "float32")]


def kernel(**inputs):
    import numpy as _np
    import concourse.bacc as _bacc
    from concourse import mybir as _mybir
    from concourse.bass_utils import run_bass_kernel_spmd as _run

    nc = _bacc.Bacc("TRN2", target_bir_lowering=False, num_devices=1)
    arrays, args = {}, []
    for name in _INS:
        a = _np.asarray(inputs[name])
        if name != "x":
            a = a.reshape(TAPS * TAPS, C).T
        a = _np.ascontiguousarray(a)
        arrays[f"in_{name}_dram"] = a
        args.append(nc.dram_tensor(f"in_{name}_dram", a.shape, _mybir.dt.from_np(a.dtype), kind="ExternalInput").ap())
    for i, (shape, dtype) in enumerate(_OUTS):
        dt = _mybir.dt.from_np(_np.dtype(dtype))
        args.append(nc.dram_tensor(f"out_{i}_dram", shape, dt, kind="ExternalOutput").ap())
    band_conv_kernel(nc, *args)
    r = _run(nc, [arrays], core_ids=[0])
    return r.results[0]["out_0_dram"]
```

```python
from contextlib import ExitStack

import concourse.bass as bass
from concourse import mybir

ALU = mybir.AluOpType
ACT = mybir.ActivationFunctionType
F32 = mybir.dt.float32
BF16 = mybir.dt.bfloat16
FP8 = mybir.dt.float8e4
U32 = mybir.dt.uint32


N, H, W, C = 16, 112, 112, 256
GROUP = 8
HALVES = 2
CH = C // HALVES
GPU = CH // GROUP
UNITS = HALVES * N
HALF_GROUPS = N * GPU
GROUPS = HALVES * HALF_GROUPS
TAPS = 3
M = 128
PITCH = 113
BANDS = CH * TAPS
GROUP_BANDS = GROUP * TAPS * PITCH
SCRATCH_W = M + BANDS * PITCH + M
COPIES = 16
PC = 128
SLOT = GROUP * PC
PIECES = 4
WP = W // PIECES
BPIECES = 4
BGROUPS = GPU // BPIECES
GUARD = M - PITCH
BPIECE_W = BGROUPS * GROUP_BANDS + GUARD
PERIOD = 2 * GPU
SUMS = 2
BY_SCALAR = (2, 4, 6, 8, 10, 12, 14)
LEAD = 3
DMA = 16


def band_conv_kernel(nc, x, k0, k1, out):
    band_rows = nc.dram_tensor("band_rows", [2 * HALVES * COPIES, SCRATCH_W], FP8, kind="Internal").ap()

    with ExitStack() as ctx:
        def sb(name, shape, dt):
            return ctx.enter_context(nc.sbuf_tensor(name, shape, dt))

        def pb(name, shape, dt):
            return ctx.enter_context(nc.psum_tensor(name, shape, dt))

        def sem(name):
            return ctx.enter_context(nc.semaphore(name))

        act_x = sb("act_x", [H, 2, W, CH], F32)
        bands = [sb(f"bands{l}", [H, BPIECES * BPIECE_W], FP8) for l in range(2)]
        signs = [sb(f"signs{l}", [H, 2, GROUP, W + 2], BF16) for l in range(2)]
        rowsum = [sb(f"rowsum{l}", [H, SUMS], F32) for l in range(2)]
        minus_mean = sb("minus_mean", [H, 1], F32)
        ones = sb("ones", [H, 1], F32)
        averager = sb("averager", [H, M], F32)
        taps = sb("taps", [CH, 2 * HALVES, TAPS * TAPS], F32)
        unread_or_taps = sb("unread_or_taps", [CH, GROUP * W], BF16)
        unread = unread_or_taps[0:H, :].rearrange("h (c w) -> h c w", c=GROUP)
        tap_rows = unread_or_taps[:, :].bitcast(FP8)[:, 0:2 * HALVES * TAPS * PITCH].rearrange(
            "c (s d t) -> c s d t", s=2 * HALVES, d=TAPS)
        zero_rows = sb("zero_rows", [2 * HALVES * COPIES, M], FP8)

        conv_ps = [pb("conv0_ps", [M, 2, GROUP, PC], F32), pb("conv1_ps", [M, 1, GROUP, PC], F32)]
        mean_ps = [pb(f"mean{l}_ps", [M, 512], F32) for l in range(2)]

        taps_loaded = sem("taps_loaded")
        zeros_set = sem("zeros_set")
        taps_signed = sem("taps_signed")
        rows_built = sem("rows_built")
        rows_stored = sem("rows_stored")
        band_loaded = [[sem(f"band{l}_loaded{q}") for q in range(BPIECES)] for l in range(2)]
        constants_set = sem("constants_set")
        loaded = sem("loaded")
        stored = [sem(f"stored{i}") for i in range(PIECES)]
        rowsum_ready = sem("rowsum_ready")
        mean_ready = [sem("mean0_ready"), sem("mean1_ready")]
        sign_ready = [sem("sign0_ready"), sem("sign1_ready")]
        mean_taken = sem("mean_taken")
        compared = sem("compared")
        scalar_signed = sem("scalar_signed")
        conv_ready = [sem("conv0_ready"), sem("conv1_ready")]
        added = [sem("added0"), sem("added1")]

        by_channel = act_x[:, :, :, :].rearrange("p u w c -> p c (u w)")

        def group_at(i):
            u, gi = divmod(i % PERIOD, GPU)
            return by_channel[:, gi * GROUP:(gi + 1) * GROUP, u * W:(u + 1) * W]

        def steps(eng, step, per_turn):
            first = 2
            last = GROUPS - LEAD - (GROUPS - LEAD - first) % per_turn
            for t in range(-LEAD, first):
                step(t, t % per_turn)
            with eng.Fori(first, last, per_turn) as t0:
                for i in range(per_turn):
                    step(t0 + i, (first + i) % per_turn)
            for t in range(last, GROUPS + 2):
                step(t, t % per_turn)

        def by_scalar(i):
            return i % GPU in BY_SCALAR

        def nth0(g, i):
            mine = [gi for gi in range(GPU) if by_scalar(gi) == by_scalar(i)]
            return g // GPU * len(mine) + mine.index(i % GPU) + 1

        block = ctx.enter_context(nc.Block())

        def valid(g):
            return not isinstance(g, int) or 0 <= g < GROUPS

        def later(g, by):
            return not isinstance(g, int) or g >= by

        @block.sync
        def _(sp):
            def piece(dram, half, n, i):
                return dram[n, :, i * WP:(i + 1) * WP, half * CH:(half + 1) * CH]

            def held(u, i):
                return act_x[:, u % 2, i * WP:(i + 1) * WP, :]

            def load(half, n, u, i):
                sp.dma_start(held(u, i), piece(x, half, n, i)).then_inc(loaded, DMA)

            def store(half, n, u, i):
                sp.dma_start(piece(out, half, n, i), held(u, i)).then_inc(stored[i], DMA)

            def turn(half, n, parity, next_half, next_n, nth):
                sp.wait_ge(added[1], (nth + 1) * GPU)
                for i in range(PIECES):
                    store(half, n, parity, i)
                if next_n is None:
                    return
                sp.wait_ge(loaded, (nth + 2) * PIECES * DMA)
                for i in range(PIECES):
                    sp.wait_ge(stored[i], (nth + 1) * DMA)
                    load(next_half, next_n, parity, i)

            for i in range(PIECES):
                load(0, 0, 0, i)
            sp.wait_ge(loaded, PIECES * DMA)
            for i in range(PIECES):
                load(0, 1, 1, i)
            for half in range(HALVES):
                with sp.Fori(0, N // 2 - 1) as pair:
                    for parity in range(2):
                        n = pair * 2 + parity
                        turn(half, n, parity, half, n + 2, n + half * N)
                for parity in range(2):
                    more = half + 1 < HALVES
                    turn(half, N - 2 + parity, parity, half + 1, parity if more else None,
                         half * N + N - 2 + parity)
            for i in range(PIECES):
                sp.wait_ge(stored[i], UNITS * DMA)

        @block.gpsimd
        def _(pool):
            nc.gpsimd.memset(ones[:, :], 1.0)
            nc.gpsimd.memset(averager[:, :], 1.0 / (H * W * GROUP))
            for l in range(2):
                for edge in (0, W + 1):
                    last = nc.gpsimd.memset(signs[l][:, :, :, edge:edge + 1], 0.0)
            last.then_inc(constants_set, 1)

            for l, k in enumerate((k0, k1)):
                pool.dma_start(taps[:, l * HALVES:(l + 1) * HALVES, :],
                               k.rearrange("(h c) t -> c h t", h=HALVES)).then_inc(taps_loaded, DMA)

            pool.wait_ge(zeros_set, 2)
            pool.dma_start(band_rows[:, 0:M], zero_rows[:, :]).then_inc(rows_stored, DMA)
            pool.dma_start(band_rows[:, SCRATCH_W - M:], zero_rows[:, :]).then_inc(rows_stored, DMA)
            pool.wait_ge(rows_built, TAPS)
            for s in range(2 * HALVES):
                pool.dma_start(
                    band_rows[s * COPIES:(s + 1) * COPIES, M:M + BANDS * PITCH].rearrange("r (c t) -> c r t", c=CH),
                    tap_rows[:, s:s + 1, :, :].rearrange("c s d t -> c s (d t)").to_broadcast(
                        [CH, COPIES, TAPS * PITCH])).then_inc(rows_stored, DMA)
            pool.wait_ge(rows_stored, (2 + 2 * HALVES) * DMA)

            def load_bands(l, half, q):
                row = l * HALVES + half
                for h in range(0, H, COPIES):
                    start = row * COPIES * SCRATCH_W + M + 1 - h + q * BGROUPS * GROUP_BANDS
                    src = bass.AP(band_rows.tensor, start, [[SCRATCH_W - 1, COPIES], [1, BPIECE_W]])
                    pool.dma_start(bands[l][h:h + COPIES, q * BPIECE_W:(q + 1) * BPIECE_W],
                                   src).then_inc(band_loaded[l][q], DMA)

            for q in range(BPIECES):
                for l in range(2):
                    load_bands(l, 0, q)
            for half in range(1, HALVES):
                before = half * HALF_GROUPS - GPU
                for q in range(BPIECES):
                    for l in range(2):
                        pool.wait_ge(conv_ready[l], before + (q + 1) * BGROUPS)
                        load_bands(l, half, q)

        @block.scalar
        def _(act):
            act.wait_ge(rows_stored, (2 + 2 * HALVES) * DMA)

            def sum_rows(g, i):
                slot = i % SUMS
                act.wait_ge(loaded, (g // GPU + 1) * PIECES * DMA)
                if later(g, SUMS):
                    act.wait_ge(mean_ready[0], g - (SUMS - 1))
                if later(g, 1):
                    act.wait_ge(rowsum_ready, g)
                nc.scalar.activation(unread, group_at(i), ACT.Copy,
                                     accum_out=rowsum[0][:, slot:slot + 1]).then_inc(rowsum_ready, 1)

            def sign(g, i):
                nth = nth0(g, i)
                s = signs[0][:, i % 2, :, 1:W + 1]
                act.wait_ge(mean_ready[0], g + 1)
                nc.scalar.activation(minus_mean[:, :], mean_ps[0][0:H, 0:1], ACT.Copy,
                                     scale=-1.0).then_inc(mean_taken, 1)
                act.wait_ge(mean_taken, nth)
                if later(g, 2):
                    act.wait_ge(conv_ready[0], g - 1)
                nc.scalar.activation(s, group_at(i), ACT.Sign, bias=minus_mean[:, :]).then_inc(compared, 1)
                act.wait_ge(compared, nth)
                nc.scalar.activation(s, s, ACT.Sign, scale=2.0, bias=ones[:, :]).then_inc(scalar_signed, 1)

            def step(t, i):
                if valid(t + 1) and by_scalar(i + 1):
                    sign(t + 1, i + 1)
                if valid(t + 3):
                    sum_rows(t + 3, i + 3)

            act.wait_ge(constants_set, 1)

            steps(act, step, PERIOD)

        @block.vector
        def _(dve):
            nc.vector.memset(zero_rows[:, :], 0.0).then_inc(zeros_set, 1)
            nc.vector.memset(tap_rows[:, :, :, :], 0.0).then_inc(zeros_set, 1)
            dve.wait_ge(taps_loaded, 2 * DMA)
            nc.vector.tensor_scalar(taps[:, :, :], taps[:, :, :], 0.0, 0.5,
                                    ALU.is_ge, ALU.subtract).then_inc(taps_signed, 1)
            dve.wait_ge(taps_signed, 1)
            dve.wait_ge(zeros_set, 2)
            for dy in range(TAPS):
                nc.vector.tensor_scalar(tap_rows[:, :, :, TAPS - 1 - dy], taps[:, :, dy * TAPS:(dy + 1) * TAPS],
                                        4.0, None, ALU.mult, saturate=False).then_inc(rows_built, 1)
            dve.wait_ge(constants_set, 1)

            def sign(l, g, i):
                dve.wait_ge(mean_ready[l], g + 1)
                if later(g, 2):
                    dve.wait_ge(conv_ready[l], g - 1)
                nc.vector.tensor_scalar(signs[l][:, i % 2, :, 1:W + 1], group_at(i), mean_ps[l][0:H, 0:1], 0.5,
                                        ALU.is_ge, ALU.subtract).then_inc(sign_ready[l], 1)

            def add(l, g, i):
                dve.wait_ge(conv_ready[l], g + 1)
                here = group_at(i)
                if l == 0:
                    scale = 0.5 if by_scalar(i) else 1.0
                    nc.vector.scalar_tensor_tensor(here, conv_ps[0][0:H, i % 2, :, 0:W], scale, here,
                                                   ALU.mult, ALU.add,
                                                   accum_out=rowsum[1][:, i % 2:i % 2 + 1]).then_inc(added[0], 1)
                else:
                    nc.vector.tensor_tensor(here, conv_ps[1][0:H, 0, :, 0:W], here, ALU.add).then_inc(added[1], 1)

            def step(t, i):
                if valid(t + 1) and not by_scalar(i + 1):
                    sign(0, t + 1, i + 1)
                if valid(t):
                    add(0, t, i)
                if valid(t - 1):
                    sign(1, t - 1, i - 1)
                if valid(t - 2):
                    add(1, t - 2, i - 2)

            steps(dve, step, PERIOD)

        @block.tensor
        def _(pe):
            pe.wait_ge(constants_set, 1)

            def wait_signed(l, g, i):
                if l == 0 and by_scalar(i):
                    pe.wait_ge(scalar_signed, nth0(g, i))
                else:
                    pe.wait_ge(sign_ready[l], nth0(g, i) if l == 0 else g + 1)

            def mean(l, g, i):
                pe.wait_ge(rowsum_ready if l == 0 else added[0], g + 1)
                if l == 0 and later(g, 1) and by_scalar(i - 1):
                    pe.wait_ge(mean_taken, nth0(g - 1, i - 1))
                elif later(g, 1):
                    wait_signed(l, g - 1, i - 1)
                nc.tensor.matmul(mean_ps[l][:, 0:1], averager[:, :], rowsum[l][:, i % SUMS:i % SUMS + 1],
                                 start=True, stop=True).then_inc(mean_ready[l], 1)

            def conv_waits(l, g, gi):
                q, in_piece = divmod(gi, BGROUPS)
                if in_piece == 0:
                    pe.wait_ge(band_loaded[l][q], (g // HALF_GROUPS + 1) * (H // COPIES) * DMA)
                slots = 2 - l
                if later(g, slots):
                    pe.wait_ge(added[l], g - slots + 1)
                wait_signed(l, g, gi)

            def take_waits(l, gi):
                some = signs[l][:, gi % 2, :, :].rearrange("p c w -> p (c w)")
                nc.tensor.matmul(conv_ps[l][:, gi % (2 - l), 0, 0:1], some[:, 0:M], some[:, 0:1],
                                 start=True, stop=True)

            def conv(l, gi):
                q, in_piece = divmod(gi, BGROUPS)
                slots = 2 - l
                for c in range(GROUP):
                    for dx in range(TAPS):
                        at = q * BPIECE_W + ((in_piece * GROUP + c) * TAPS + dx) * PITCH
                        last = nc.tensor.matmul(
                            conv_ps[l][:, gi % slots, c, 0:W],
                            bands[l][:, at:at + M],
                            signs[l][:, gi % 2, c, dx:dx + W],
                            start=(dx == 0), stop=(dx == TAPS - 1))
                last.then_inc(conv_ready[l], 1)

            def step(t, i):
                if valid(t + 1) and (i + 1) % GPU == 0:
                    mean(0, t + 1, i + 1)
                if valid(t - 2):
                    conv_waits(1, t - 2, (i - 2) % GPU)
                if valid(t - 1):
                    mean(1, t - 1, i - 1)
                if valid(t - 2):
                    conv(1, (i - 2) % GPU)
                if valid(t + 1):
                    conv_waits(0, t + 1, (i + 1) % GPU)
                if valid(t + 2) and (i + 2) % GPU > 0:
                    mean(0, t + 2, i + 2)
                elif valid(t + 1):
                    take_waits(0, (i + 1) % GPU)
                if valid(t + 1):
                    conv(0, (i + 1) % GPU)

            steps(pe, step, GPU)


_INS = ["x", "L0_conv_kernel", "L1_conv_kernel"]
_OUTS = [((N, H, W, C), "float32")]


def kernel(**inputs):
    import numpy as _np
    import concourse.bacc as _bacc
    from concourse import mybir as _mybir
    from concourse.bass_utils import run_bass_kernel_spmd as _run

    nc = _bacc.Bacc("TRN2", target_bir_lowering=False, num_devices=1)
    arrays, args = {}, []
    for name in _INS:
        a = _np.asarray(inputs[name])
        if name != "x":
            a = a.reshape(TAPS * TAPS, C).T
        a = _np.ascontiguousarray(a)
        arrays[f"in_{name}_dram"] = a
        args.append(nc.dram_tensor(f"in_{name}_dram", a.shape, _mybir.dt.from_np(a.dtype), kind="ExternalInput").ap())
    for i, (shape, dtype) in enumerate(_OUTS):
        dt = _mybir.dt.from_np(_np.dtype(dtype))
        args.append(nc.dram_tensor(f"out_{i}_dram", shape, dt, kind="ExternalOutput").ap())
    band_conv_kernel(nc, *args)
    r = _run(nc, [arrays], core_ids=[0])
    return r.results[0]["out_0_dram"]
```

```python
from contextlib import ExitStack

import concourse.bass as bass
from concourse import mybir

ALU = mybir.AluOpType
ACT = mybir.ActivationFunctionType
F32 = mybir.dt.float32
BF16 = mybir.dt.bfloat16
FP8 = mybir.dt.float8e4
U32 = mybir.dt.uint32


N, H, W, C = 16, 112, 112, 256
GROUP = 8
HALVES = 2
CH = C // HALVES
GPU = CH // GROUP
UNITS = HALVES * N
HALF_GROUPS = N * GPU
GROUPS = HALVES * HALF_GROUPS
TAPS = 3
M = 128
PITCH = 113
BANDS = CH * TAPS
GROUP_BANDS = GROUP * TAPS * PITCH
SCRATCH_W = M + BANDS * PITCH + M
COPIES = 16
PC = 128
PIECES = 4
WP = W // PIECES
BPIECES = 4
BGROUPS = GPU // BPIECES
GUARD = M - PITCH
BPIECE_W = BGROUPS * GROUP_BANDS + GUARD
PERIOD = 2 * GPU
SUMS = 2
BY_SCALAR = (2, 4, 6, 8, 10, 12, 14)
LEAD = 3
DMA = 16


def band_conv_kernel(nc, x, k0, k1, out):
    band_rows = nc.dram_tensor("band_rows", [2 * HALVES * COPIES, SCRATCH_W], FP8, kind="Internal").ap()

    with ExitStack() as ctx:
        def sb(name, shape, dt):
            return ctx.enter_context(nc.sbuf_tensor(name, shape, dt))

        def pb(name, shape, dt):
            return ctx.enter_context(nc.psum_tensor(name, shape, dt))

        def sem(name):
            return ctx.enter_context(nc.semaphore(name))

        units = sb("units", [CH, 2, W, CH], F32)
        act_x = units[0:H, :, :, :]
        tap_rows = units[:, 1, 0:W // 2, :].rearrange("p w c -> p (w c)").bitcast(FP8)[
            :, 0:2 * HALVES * TAPS * PITCH].rearrange("c (s d t) -> c s d t", s=2 * HALVES, d=TAPS)
        bands = [sb(f"bands{l}", [H, BPIECES * BPIECE_W], FP8) for l in range(2)]
        signs = [sb(f"signs{l}", [H, 2, GROUP, W + 2], BF16) for l in range(2)]
        rowsum = [sb(f"rowsum{l}", [H, SUMS], F32) for l in range(2)]
        minus_mean = sb("minus_mean", [H, 1], F32)
        ones = sb("ones", [H, 1], F32)
        averager = sb("averager", [H, M], F32)
        taps = sb("taps", [CH, HALVES, 2, TAPS * TAPS], F32)
        unread = sb("unread", [H, GROUP, W], BF16)
        zero_rows = sb("zero_rows", [2 * HALVES * COPIES, M], FP8)

        conv_ps = [pb("conv0_ps", [M, 2, GROUP, PC], F32), pb("conv1_ps", [M, 1, GROUP, PC], F32)]
        mean_ps = [pb(f"mean{l}_ps", [M, 512], F32) for l in range(2)]

        taps_loaded = sem("taps_loaded")
        zeros_set = sem("zeros_set")
        taps_signed = sem("taps_signed")
        rows_built = sem("rows_built")
        rows_stored = [sem(f"rows_stored{half}") for half in range(HALVES)]
        band_loaded = [[sem(f"band{l}_loaded{q}") for q in range(BPIECES)] for l in range(2)]
        constants_set = sem("constants_set")
        loaded = sem("loaded")
        stored = [sem(f"stored{i}") for i in range(PIECES)]
        rowsum_ready = sem("rowsum_ready")
        mean_ready = [sem("mean0_ready"), sem("mean1_ready")]
        sign_ready = [sem("sign0_ready"), sem("sign1_ready")]
        mean_taken = sem("mean_taken")
        compared = sem("compared")
        scalar_signed = sem("scalar_signed")
        conv_ready = [sem("conv0_ready"), sem("conv1_ready")]
        added = [sem("added0"), sem("added1")]

        by_channel = act_x[:, :, :, :].rearrange("p u w c -> p c (u w)")

        def group_at(i):
            u, gi = divmod(i % PERIOD, GPU)
            return by_channel[:, gi * GROUP:(gi + 1) * GROUP, u * W:(u + 1) * W]

        def steps(eng, step, per_turn):
            first = 2
            last = GROUPS - LEAD - (GROUPS - LEAD - first) % per_turn
            for t in range(-LEAD, first):
                step(t, t % per_turn)
            with eng.Fori(first, last, per_turn) as t0:
                for i in range(per_turn):
                    step(t0 + i, (first + i) % per_turn)
            for t in range(last, GROUPS + 2):
                step(t, t % per_turn)

        def by_scalar(i):
            return i % GPU in BY_SCALAR

        def nth0(g, i):
            mine = [gi for gi in range(GPU) if by_scalar(gi) == by_scalar(i)]
            return g // GPU * len(mine) + mine.index(i % GPU) + 1

        def load_bands(eng, l, half, q):
            row = half * 2 + l
            for h in range(0, H, COPIES):
                start = row * COPIES * SCRATCH_W + M + 1 - h + q * BGROUPS * GROUP_BANDS
                src = bass.AP(band_rows.tensor, start, [[SCRATCH_W - 1, COPIES], [1, BPIECE_W]])
                eng.dma_start(bands[l][h:h + COPIES, q * BPIECE_W:(q + 1) * BPIECE_W],
                              src).then_inc(band_loaded[l][q], DMA)

        def reload_bands(eng, l, half, q):
            eng.wait_ge(conv_ready[l], half * HALF_GROUPS - GPU + (q + 1) * BGROUPS)
            load_bands(eng, l, half, q)

        block = ctx.enter_context(nc.Block())

        def valid(g):
            return not isinstance(g, int) or 0 <= g < GROUPS

        def later(g, by):
            return not isinstance(g, int) or g >= by

        @block.sync
        def _(sp):
            def piece(dram, half, n, i):
                return dram[n, :, i * WP:(i + 1) * WP, half * CH:(half + 1) * CH]

            def held(u, i):
                return act_x[:, u % 2, i * WP:(i + 1) * WP, :]

            def load(half, n, u, i):
                sp.dma_start(held(u, i), piece(x, half, n, i)).then_inc(loaded, DMA)

            def store(half, n, u, i):
                sp.dma_start(piece(out, half, n, i), held(u, i)).then_inc(stored[i], DMA)

            def turn(half, n, parity, next_half, next_n, nth):
                sp.wait_ge(added[1], (nth + 1) * GPU)
                for i in range(PIECES):
                    store(half, n, parity, i)
                if next_n is None:
                    return
                sp.wait_ge(loaded, (nth + 2) * PIECES * DMA)
                for i in range(PIECES):
                    sp.wait_ge(stored[i], (nth + 1) * DMA)
                    load(next_half, next_n, parity, i)

            def store_rows(half):
                for s in (half * 2, half * 2 + 1):
                    sp.dma_start(
                        band_rows[s * COPIES:(s + 1) * COPIES, M:M + BANDS * PITCH].rearrange(
                            "r (c t) -> c r t", c=CH),
                        tap_rows[:, s:s + 1, :, :].rearrange("c s d t -> c s (d t)").to_broadcast(
                            [CH, COPIES, TAPS * PITCH])).then_inc(rows_stored[half], DMA)

            for l, k in enumerate((k0, k1)):
                sp.dma_start(taps[:, :, l, :], k.rearrange("(h c) t -> c h t", h=HALVES)).then_inc(taps_loaded, DMA)
            load(0, 0, 0, 0)
            load(0, 0, 0, 1)
            sp.wait_ge(zeros_set, 2)
            sp.dma_start(band_rows[:, 0:M], zero_rows[:, :]).then_inc(rows_stored[0], DMA)
            sp.dma_start(band_rows[:, SCRATCH_W - M:], zero_rows[:, :]).then_inc(rows_stored[0], DMA)
            sp.wait_ge(rows_built, TAPS)
            store_rows(0)
            for i in range(2, PIECES):
                load(0, 0, 0, i)
            sp.wait_ge(rows_stored[0], (2 + 2) * DMA)
            load_bands(sp, 0, 0, 0)
            store_rows(1)
            for q in range(1, BPIECES):
                load_bands(sp, 0, 0, q)
            sp.wait_ge(loaded, PIECES * DMA)
            sp.wait_ge(rows_stored[1], 2 * DMA)
            for i in range(PIECES):
                load(0, 1, 1, i)
            for half in range(HALVES):
                with sp.Fori(0, N // 2 - 1) as pair:
                    for parity in range(2):
                        n = pair * 2 + parity
                        turn(half, n, parity, half, n + 2, n + half * N)
                for parity in range(2):
                    more = half + 1 < HALVES
                    turn(half, N - 2 + parity, parity, half + 1, parity if more else None,
                         half * N + N - 2 + parity)
                    if more and parity == 0:
                        for q in range(BPIECES):
                            reload_bands(sp, 0, half + 1, q)
            for i in range(PIECES):
                sp.wait_ge(stored[i], UNITS * DMA)

        @block.gpsimd
        def _(pool):
            nc.gpsimd.memset(ones[:, :], 1.0)
            nc.gpsimd.memset(averager[:, :], 1.0 / (H * W * GROUP))
            for l in range(2):
                for edge in (0, W + 1):
                    last = nc.gpsimd.memset(signs[l][:, :, :, edge:edge + 1], 0.0)
            last.then_inc(constants_set, 1)

            pool.wait_ge(rows_stored[0], (2 + 2) * DMA)
            for q in range(BPIECES):
                load_bands(pool, 1, 0, q)
            for half in range(1, HALVES):
                pool.wait_ge(rows_stored[half], 2 * DMA)
                for q in range(BPIECES):
                    reload_bands(pool, 1, half, q)

        @block.scalar
        def _(act):
            def sum_rows(g, i):
                slot = i % SUMS
                act.wait_ge(loaded, (g // GPU + 1) * PIECES * DMA)
                if later(g, SUMS):
                    act.wait_ge(mean_ready[0], g - (SUMS - 1))
                if later(g, 1):
                    act.wait_ge(rowsum_ready, g)
                nc.scalar.activation(unread[:, :, :], group_at(i), ACT.Copy,
                                     accum_out=rowsum[0][:, slot:slot + 1]).then_inc(rowsum_ready, 1)

            def sign(g, i):
                nth = nth0(g, i)
                s = signs[0][:, i % 2, :, 1:W + 1]
                act.wait_ge(mean_ready[0], g + 1)
                nc.scalar.activation(minus_mean[:, :], mean_ps[0][0:H, 0:1], ACT.Copy,
                                     scale=-1.0).then_inc(mean_taken, 1)
                act.wait_ge(mean_taken, nth)
                if later(g, 2):
                    act.wait_ge(conv_ready[0], g - 1)
                nc.scalar.activation(s, group_at(i), ACT.Sign, bias=minus_mean[:, :]).then_inc(compared, 1)
                act.wait_ge(compared, nth)
                nc.scalar.activation(s, s, ACT.Sign, scale=2.0, bias=ones[:, :]).then_inc(scalar_signed, 1)

            def step(t, i):
                if valid(t + 1) and by_scalar(i + 1):
                    sign(t + 1, i + 1)
                if valid(t + 3):
                    sum_rows(t + 3, i + 3)

            act.wait_ge(constants_set, 1)

            steps(act, step, PERIOD)

        @block.vector
        def _(dve):
            nc.vector.memset(zero_rows[:, :], 0.0).then_inc(zeros_set, 1)
            nc.vector.memset(tap_rows[:, :, :, :], 0.0).then_inc(zeros_set, 1)
            dve.wait_ge(taps_loaded, 2 * DMA)
            nc.vector.tensor_scalar(taps[:, :, :, :], taps[:, :, :, :], 0.0, 0.5,
                                    ALU.is_ge, ALU.subtract).then_inc(taps_signed, 1)
            dve.wait_ge(taps_signed, 1)
            dve.wait_ge(zeros_set, 2)
            for dy in range(TAPS):
                nc.vector.tensor_scalar(tap_rows[:, :, :, TAPS - 1 - dy],
                                        taps[:, :, :, dy * TAPS:(dy + 1) * TAPS].rearrange("c h l d -> c (h l) d"),
                                        4.0, None, ALU.mult, saturate=False).then_inc(rows_built, 1)
            dve.wait_ge(constants_set, 1)

            def sign(l, g, i):
                dve.wait_ge(mean_ready[l], g + 1)
                if later(g, 2):
                    dve.wait_ge(conv_ready[l], g - 1)
                nc.vector.tensor_scalar(signs[l][:, i % 2, :, 1:W + 1], group_at(i), mean_ps[l][0:H, 0:1], 0.5,
                                        ALU.is_ge, ALU.subtract).then_inc(sign_ready[l], 1)

            def add(l, g, i):
                dve.wait_ge(conv_ready[l], g + 1)
                here = group_at(i)
                if l == 0:
                    scale = 0.5 if by_scalar(i) else 1.0
                    nc.vector.scalar_tensor_tensor(here, conv_ps[0][0:H, i % 2, :, 0:W], scale, here,
                                                   ALU.mult, ALU.add,
                                                   accum_out=rowsum[1][:, i % 2:i % 2 + 1]).then_inc(added[0], 1)
                else:
                    nc.vector.tensor_tensor(here, conv_ps[1][0:H, 0, :, 0:W], here, ALU.add).then_inc(added[1], 1)

            def step(t, i):
                if valid(t + 1) and not by_scalar(i + 1):
                    sign(0, t + 1, i + 1)
                if valid(t):
                    add(0, t, i)
                if valid(t - 1):
                    sign(1, t - 1, i - 1)
                if valid(t - 2):
                    add(1, t - 2, i - 2)

            steps(dve, step, PERIOD)

        @block.tensor
        def _(pe):
            pe.wait_ge(constants_set, 1)

            def wait_signed(l, g, i):
                if l == 0 and by_scalar(i):
                    pe.wait_ge(scalar_signed, nth0(g, i))
                else:
                    pe.wait_ge(sign_ready[l], nth0(g, i) if l == 0 else g + 1)

            def mean(l, g, i):
                pe.wait_ge(rowsum_ready if l == 0 else added[0], g + 1)
                if l == 0 and later(g, 1) and by_scalar(i - 1):
                    pe.wait_ge(mean_taken, nth0(g - 1, i - 1))
                elif later(g, 1):
                    wait_signed(l, g - 1, i - 1)
                nc.tensor.matmul(mean_ps[l][:, 0:1], averager[:, :], rowsum[l][:, i % SUMS:i % SUMS + 1],
                                 start=True, stop=True).then_inc(mean_ready[l], 1)

            def conv_waits(l, g, gi):
                q, in_piece = divmod(gi, BGROUPS)
                if in_piece == 0:
                    pe.wait_ge(band_loaded[l][q], (g // HALF_GROUPS + 1) * (H // COPIES) * DMA)
                slots = 2 - l
                if later(g, slots):
                    pe.wait_ge(added[l], g - slots + 1)
                wait_signed(l, g, gi)

            def take_waits(l, gi):
                some = signs[l][:, gi % 2, :, :].rearrange("p c w -> p (c w)")
                nc.tensor.matmul(conv_ps[l][:, gi % (2 - l), 0, 0:1], some[:, 0:M], some[:, 0:1],
                                 start=True, stop=True)

            def conv(l, gi):
                q, in_piece = divmod(gi, BGROUPS)
                slots = 2 - l
                for c in range(GROUP):
                    for dx in range(TAPS):
                        at = q * BPIECE_W + ((in_piece * GROUP + c) * TAPS + dx) * PITCH
                        last = nc.tensor.matmul(
                            conv_ps[l][:, gi % slots, c, 0:W],
                            bands[l][:, at:at + M],
                            signs[l][:, gi % 2, c, dx:dx + W],
                            start=(dx == 0), stop=(dx == TAPS - 1))
                last.then_inc(conv_ready[l], 1)

            def step(t, i):
                if valid(t + 1) and (i + 1) % GPU == 0:
                    mean(0, t + 1, i + 1)
                if valid(t - 2):
                    conv_waits(1, t - 2, (i - 2) % GPU)
                if valid(t - 1):
                    mean(1, t - 1, i - 1)
                if valid(t - 2):
                    conv(1, (i - 2) % GPU)
                if valid(t + 1):
                    conv_waits(0, t + 1, (i + 1) % GPU)
                if valid(t + 2) and (i + 2) % GPU > 0:
                    mean(0, t + 2, i + 2)
                elif valid(t + 1):
                    take_waits(0, (i + 1) % GPU)
                if valid(t + 1):
                    conv(0, (i + 1) % GPU)

            steps(pe, step, GPU)


_INS = ["x", "L0_conv_kernel", "L1_conv_kernel"]
_OUTS = [((N, H, W, C), "float32")]


def kernel(**inputs):
    import numpy as _np
    import concourse.bacc as _bacc
    from concourse import mybir as _mybir
    from concourse.bass_utils import run_bass_kernel_spmd as _run

    nc = _bacc.Bacc("TRN2", target_bir_lowering=False, num_devices=1)
    arrays, args = {}, []
    for name in _INS:
        a = _np.asarray(inputs[name])
        if name != "x":
            a = a.reshape(TAPS * TAPS, C).T
        a = _np.ascontiguousarray(a)
        arrays[f"in_{name}_dram"] = a
        args.append(nc.dram_tensor(f"in_{name}_dram", a.shape, _mybir.dt.from_np(a.dtype), kind="ExternalInput").ap())
    for i, (shape, dtype) in enumerate(_OUTS):
        dt = _mybir.dt.from_np(_np.dtype(dtype))
        args.append(nc.dram_tensor(f"out_{i}_dram", shape, dt, kind="ExternalOutput").ap())
    band_conv_kernel(nc, *args)
    r = _run(nc, [arrays], core_ids=[0])
    return r.results[0]["out_0_dram"]
```
